# Optimizing a Trainium2 kernel written in Bass

```python
import numpy as np
import jax
import jax.numpy as jnp

def _softmax(x, axis=-1):
    return jax.nn.softmax(x, axis=axis)

def _gelu(x):
    return jax.nn.gelu(x, approximate=True)

def _silu(x):
    return jax.nn.silu(x)

def _sigmoid(x):
    return jax.nn.sigmoid(x)

def _layernorm(x, axis=-1, eps=1e-05):
    m = jnp.mean(x, axis=axis, keepdims=True)
    v = jnp.var(x, axis=axis, keepdims=True)
    return (x - m) / jnp.sqrt(v + eps)

def _scatter_add(tgt, idx, src, axis=0):
    return tgt.at[idx].add(src)

def _segment_sum(src, seg, n):
    return jax.ops.segment_sum(src, seg, n)
kernel_name = 'mk_adj_resnorm_d2_adj_r2_586d00'

def setup_inputs(seed: int=0):
    np.random.seed(seed)
    _w = jnp.asarray

    def _rec_inputs():
        import jax
        import jax.numpy as jnp
        _gk = jax.random.key(seed)
        x = -0.000929 + 1 * jax.random.normal(jax.random.fold_in(_gk, 1), (8192, 64), jnp.float32)
        _w = (1.0 + jnp.arange(8192, dtype=jnp.float32)) ** (-0.5)
        _w = _w / _w.mean()
        _pij = jnp.clip(0.000244141 * _w[:, None] * _w[None, :], 0.0, 1.0)
        _a = jax.random.uniform(jax.random.fold_in(_gk, 2), (8192, 8192)) < _pij
        _a = jnp.logical_or(_a, jnp.eye(8192, dtype=bool))
        _af = _a.astype(jnp.float32)
        _af = _af * jax.random.uniform(jax.random.fold_in(_gk, 3), (8192, 8192), jnp.float32, 0.05, 1)
        adj = _af
        return (x, adj)
    x, adj = _rec_inputs()

    def _L0_gnn_setup():
        import jax, jax.numpy as jnp
        import numpy as np
        P_DROP = 0.1
        key = jax.random.key(seed)
        k1, k2, k3 = jax.random.split(key, 3)
        N, D = (8192, 64)
        x = jax.random.normal(k1, (N, D), dtype=jnp.float32)
        adj = jax.random.uniform(k2, (N, N), dtype=jnp.float32)
        u = jax.random.uniform(k3, (N, D), dtype=jnp.float32)
        return {'x': x, 'adj': adj, 'u': u}
    _L0_gnn_all = _L0_gnn_setup()
    _L0_gnn_in = {k: v for k, v in _L0_gnn_all.items() if k in ('u',)}
    del _L0_gnn_all

    def _L1_gnn_setup():
        import jax, jax.numpy as jnp
        import numpy as np
        N = 5000
        DIN = 64
        DOUT = 64
        key = jax.random.key(seed)
        kx, ka, kw = jax.random.split(key, 3)
        x = jax.random.normal(kx, (N, DIN), dtype=jnp.float32)
        u = jax.random.uniform(ka, (N, N), dtype=jnp.float32)
        adj = (u < 0.01).astype(jnp.float32)
        adj = jnp.maximum(adj, adj.T) * (1.0 - jnp.eye(N, dtype=jnp.float32))
        W = jax.random.normal(kw, (DIN, DOUT), dtype=jnp.float32) * (1.0 / np.sqrt(DIN))
        b = jnp.zeros((DOUT,), dtype=jnp.float32)
        return {'x': x, 'adj_matrix': adj, 'W': W, 'b': b}
    _L1_gnn_all = _L1_gnn_setup()
    _L1_gnn_in = {k: v for k, v in _L1_gnn_all.items() if k in ('W', 'b')}
    del _L1_gnn_all
    return {'x': x, 'adj': adj, 'L0_gnn_u': _L0_gnn_in['u'], 'L1_gnn_W': _L1_gnn_in['W'], 'L1_gnn_b': _L1_gnn_in['b']}

def reference(x, adj, L0_gnn_u, L1_gnn_W, L1_gnn_b):
    import jax
    import jax.numpy as jnp

    def _L0_gnn_ref(x, adj, u):
        import jax, jax.numpy as jnp
        import numpy as np
        P_DROP = 0.1
        keep = (u >= P_DROP).astype(x.dtype)
        x_drop = x * keep / (1.0 - P_DROP)
        return jnp.matmul(adj, x_drop)

    def _L1_gnn_ref(x, adj_matrix, W, b):
        import jax, jax.numpy as jnp
        import numpy as np
        N = 5000
        DIN = 64
        DOUT = 64
        n = adj_matrix.shape[0]
        a = adj_matrix + jnp.eye(n, dtype=adj_matrix.dtype)
        degree = jnp.sum(a, axis=1)
        d_is = jnp.power(degree, -0.5)
        d_is = jnp.where(jnp.isinf(d_is), 0.0, d_is)
        a_norm = d_is[:, None] * a * d_is[None, :]
        h = x @ W + b
        out = jnp.maximum(a_norm @ h, 0.0)
        return out
    x = _layernorm(x + _L0_gnn_ref(x, adj, L0_gnn_u), axis=-1)
    x = _layernorm(x + _L1_gnn_ref(x, adj, L1_gnn_W, L1_gnn_b), axis=-1)
    return x

_drawn_inputs = setup_inputs


def setup_inputs(seed=0):
    import zlib

    import numpy as np

    out = dict(_drawn_inputs(seed))
    spreads = {'L1_gnn_b': (0.0, 0.1)}
    factors = {}
    for name, (base, spread) in spreads.items():
        noise = np.random.default_rng([zlib.crc32(name.encode()), seed]).standard_normal(out[name].shape)
        drawn = base * np.exp(spread * noise) if base else spread * noise
        out[name] = jnp.asarray(drawn.astype(out[name].dtype))
    for name, factor in factors.items():
        out[name] = (out[name] * factor).astype(out[name].dtype)
    return out
```

```python
import concourse.bass as bass
from concourse import mybir
from contextlib import ExitStack
import numpy as np


def two_layer_graph_resnorm(nc, x, adj, u, w, b, out):
    fp32 = mybir.dt.float32
    fp32r = mybir.dt.float32r
    ALU = mybir.AluOpType
    ACT = mybir.ActivationFunctionType
    AX = mybir.AxisListType

    P = 128
    N, D = x.shape
    KEEP_FROM = 0.1
    UNDROP = float(np.float32(1.0) / np.float32(0.9))
    EPS = 1e-5

    ROWS = 512
    BLOCKS = N // ROWS
    LAST = 2 * BLOCKS - 1
    S = ROWS // P
    KT = N // P
    CHUNK = 1024
    CHUNKS = N // CHUNK
    SLOTS = 4
    PER_SLOT = CHUNKS // SLOTS
    KC = CHUNK // P
    GROUPS = [[0], [1]] + [[k, k + 1] for k in range(2, KT, 2)]
    NG = len(GROUPS)
    BUFS = 3
    assert NG % BUFS == 0
    FOLD_AT, TURN_AT, PROJECT_AT = 4, 16, 21
    EVICT_AT = 2
    PREP = 8
    PT = KT // PREP

    x_rows = x.rearrange("(t p) d -> p t d", p=P)
    u_rows = u.rearrange("(t p) d -> p t d", p=P)

    ctx = ExitStack()
    with ctx:
        def sb(name, shape, dt=fp32):
            return ctx.enter_context(nc.sbuf_tensor(name, shape, dt))

        def ps(name, shape, dt=fp32):
            return ctx.enter_context(nc.psum_tensor(name, shape, dt))

        def sem(name):
            return ctx.enter_context(nc.semaphore(name))

        ring = sb("adj_ring", [P, SLOTS, S, CHUNK])
        rhs0 = sb("rhs_layer0", [P, KT, 2 * D], fp32r)
        rhs1 = sb("rhs_layer1", [P, KT, 2 * D], fp32r)
        rhs1_f = rhs1[:].bitcast(fp32)
        xt = sb("x_table", [P, KT, D])
        drop = sb("x_dropped", [P, KT, D])
        a_hi = sb("adj_hi", [P, BUFS, 2, ROWS], fp32r)
        a_hi_f = a_hi[:].bitcast(fp32)
        a_lo = sb("adj_lo", [P, BUFS, 2, ROWS], fp32r)
        acc_sb = sb("acc_sb", [P, ROWS])
        ident = sb("ident", [P, P])
        fold0 = sb("fold0", [P, D + 1])
        fold1 = sb("fold1", [P, D])
        wb = sb("w_and_b", [D + 1, D])
        pre = sb("pre_norm", [P, S, D])
        cen = sb("centred", [P, S, D])
        sq = sb("squared", [P, S, D])
        normed = sb("normed", [P, S, D])
        hd = sb("h_scaled", [P, S, D])
        x1T = sb("x1_turned", [D + 1, ROWS])
        d_all = sb("d_table", [P, KT])
        rsum, mean, vsum, var, rstd, deg, iszero, degs, dpow, nonzero, dnow = (
            sb(n, [P, S]) for n in ("rsum", "mean", "vsum", "var", "rstd", "deg", "iszero", "degs", "dpow",
                                    "nonzero", "dnow"))
        minus_half, per_column, eps = (sb(n, [P, S]) for n in ("minus_half", "per_column", "eps"))

        turn_ps = [ps(f"turned{i}", [P, 2, ROWS]) for i in range(BUFS)]
        acc = ps("acc", [P, ROWS])
        epi = ps("epi", [P, ROWS])
        z0 = epi[:, 0:S * (D + 1)].rearrange("p (s d) -> p s d", s=S)
        z1 = epi[:, 0:S * D].rearrange("p (s d) -> p s d", s=S)

        x_in = [sem(f"x_in{i}") for i in range(PREP)]
        w_in = sem("w_in")
        adj_in = [sem(f"adj_in{i}") for i in range(SLOTS)]
        out_stored = sem("out_stored")
        consts_made = sem("consts_made")
        ones_made = sem("ones_made")
        drop_made = sem("drop_made")
        rhs0_hi = sem("rhs0_hi")
        rhs0_lo = sem("rhs0_lo")
        turned = sem("turned")
        hi_made = sem("hi_made")
        lo_made = sem("lo_made")
        multiplied = sem("multiplied")
        acc_out = sem("acc_out")
        folded = sem("folded")
        pre_made = sem("pre_made")
        sums_made = sem("sums_made")
        cen_made = sem("cen_made")
        vsums_made = sem("vsums_made")
        normed_made = sem("normed_made")
        x1_turned = sem("x1_turned")
        x1T_made = sem("x1T_made")
        projected = sem("projected")
        d_made = sem("d_made")
        hd_made = sem("hd_made")
        rhs1_hi = sem("rhs1_hi")
        rhs1_made = sem("rhs1_made")
        scaled = sem("scaled")
        relu_made = sem("relu_made")
        x1_kept = sem("x1_kept")
        pool_step = sem("pool_step")

        def blocks(eng, body):
            body(0, 0, None)
            with eng.Fori(1, BLOCKS) as i:
                body(i, 0, 0)
            body(BLOCKS, 1, 0)
            with eng.Fori(BLOCKS + 1, LAST) as i:
                body(i, 1, 1)
            body(LAST, 1, 1)

        block = ctx.enter_context(nc.Block())

        @block.sync
        def _(sp):
            def load_adj(blk, layer, c):
                row0 = (blk - layer * BLOCKS) * ROWS
                src = adj[bass.ds(row0, ROWS), c * CHUNK:(c + 1) * CHUNK].rearrange("(s p) j -> p s j", p=P)
                sp.dma_start(ring[:, c % SLOTS, :, :], src).then_inc(adj_in[c % SLOTS], 16)

            def groups_through(c):
                return next(g for g, ks in enumerate(GROUPS) if ks[-1] == (c + 1) * KC - 1) + 1

            def body(blk, layer, before):
                for c in range(CHUNKS):
                    if c >= SLOTS:
                        sp.wait_ge(turned, blk * NG + groups_through(c - SLOTS))
                    elif before is not None:
                        sp.wait_ge(turned, (blk - 1) * NG + groups_through(c - SLOTS + CHUNKS))
                    load_adj(blk, layer, c)
                    if c == CHUNKS - 1 and layer == 1 and before == 1:
                        store(blk - 1)

            def store(blk):
                sp.wait_ge(normed_made, blk + 1)
                row0 = (blk - BLOCKS) * ROWS
                sp.dma_start(out[bass.ds(row0, ROWS), :].rearrange("(s p) d -> p s d", p=P),
                             normed[:]).then_inc(out_stored, 16)

            for i in range(PREP):
                piece = slice(i * PT, (i + 1) * PT)
                sp.dma_start(xt[:, piece, :], x_rows[:, piece, :]).then_inc(x_in[i], 16)
                sp.dma_start(drop[:, piece, :], u_rows[:, piece, :]).then_inc(x_in[i], 16)
                if i == 0:
                    load_adj(0, 0, 0)
            sp.dma_start(wb[0:D, :], w).then_inc(w_in, 16)
            sp.dma_start(wb[D:D + 1, :], b.rearrange("(o d) -> o d", o=1)).then_inc(w_in, 16)
            for c in range(1, CHUNKS):
                if c >= SLOTS:
                    sp.wait_ge(turned, groups_through(c - SLOTS))
                load_adj(0, 0, c)
            with sp.Fori(1, BLOCKS) as i:
                body(i, 0, 0)
            body(BLOCKS, 1, 0)
            with sp.Fori(BLOCKS + 1, LAST) as i:
                body(i, 1, 1)
            body(LAST, 1, 1)
            store(LAST)
            sp.wait_ge(out_stored, 16 * BLOCKS)

        @block.tensor
        def _(pe):
            def turn(blk, g):
                k0, k1 = GROUPS[g][0], GROUPS[g][-1]
                if k0 % KC == 0:
                    c = k0 // KC
                    pe.wait_ge(adj_in[c % SLOTS], (blk * PER_SLOT + c // SLOTS + 1) * 16)
                for k in range(k0, k1 + 1):
                    col = (k % KC) * P
                    for s in range(S):
                        last = nc.tensor.transpose(turn_ps[g % BUFS][:, k - k0, s * P:(s + 1) * P],
                                                   ring[:, (k // KC) % SLOTS, s, col:col + P], ident[:])
                last.then_inc(turned, 1)

            def multiply(blk, layer, g):
                rhs = rhs1 if layer else rhs0
                pe.wait_ge(lo_made, blk * NG + g + 1)
                ks = GROUPS[g]
                for n, k in enumerate(ks):
                    for part in (a_hi, a_lo):
                        last = nc.tensor.matmul(acc[:], rhs[:, k, :], part[:, g % BUFS, n, :],
                                                start=(k == 0 and part is a_hi),
                                                stop=(k == KT - 1 and part is a_lo))
                last.then_inc(multiplied, 1)

            def fold(blk, layer):
                f = fold1 if layer else fold0
                width = D if layer else D + 1
                pe.wait_ge(acc_out, blk + 1)
                for s in range(S):
                    last = nc.tensor.matmul(epi[:, s * width:(s + 1) * width], acc_sb[:, s * P:(s + 1) * P], f[:],
                                            start=True, stop=True)
                last.then_inc(folded, 1)

            def turn_x1(blk):
                for s in range(S):
                    last = nc.tensor.transpose(epi[0:D, s * P:(s + 1) * P], normed[:, s, :], ident[:])
                last.then_inc(x1_turned, 1)

            def project(blk):
                pe.wait_ge(x1T_made, blk + 1)
                for s in range(S):
                    last = nc.tensor.matmul(epi[:, s * D:(s + 1) * D], x1T[:, s * P:(s + 1) * P], wb[:],
                                            start=True, stop=True)
                last.then_inc(projected, 1)

            pe.wait_ge(ones_made, 1)
            pe.wait_ge(consts_made, 4)
            pe.wait_ge(w_in, 32)
            turn(0, 0)
            turn(0, 1)

            def body(blk, layer, before):
                for g in range(NG):
                    if g + 2 < NG:
                        turn(blk, g + 2)
                    elif not (isinstance(blk, int) and blk == LAST):
                        turn(blk + 1, g + 2 - NG)
                    if before is None and GROUPS[g][0] % PT == 0:
                        pe.wait_ge(rhs0_lo, GROUPS[g][0] // PT + 1)
                    if before is not None and g == 0:
                        pe.wait_ge(acc_out, blk)
                        if layer == 1 and before == 0:
                            pe.wait_ge(rhs1_made, BLOCKS - 1)
                    if layer == 1 and before == 0 and GROUPS[g][0] == KT - S:
                        pe.wait_ge(rhs1_made, BLOCKS)
                    if before == 0 and g == TURN_AT:
                        pe.wait_ge(normed_made, blk)
                    multiply(blk, layer, g)
                    if before is None:
                        continue
                    if g == FOLD_AT:
                        fold(blk - 1, before)
                    if before == 0 and g == TURN_AT:
                        turn_x1(blk - 1)
                    if before == 0 and g == PROJECT_AT:
                        project(blk - 1)

            blocks(pe, body)
            fold(LAST, 1)

        @block.scalar
        def _(act):
            def evict(blk):
                act.wait_ge(multiplied, (blk + 1) * NG)
                nc.scalar.activation(acc_sb[:], acc[:], ACT.Copy).then_inc(acc_out, 1)

            def body(blk, layer, before):
                for g in range(NG):
                    n = len(GROUPS[g])
                    if before is not None and g == EVICT_AT:
                        evict(blk - 1)
                    act.wait_ge(turned, blk * NG + g + 1)
                    if g >= BUFS:
                        act.wait_ge(multiplied, blk * NG + g - BUFS + 1)
                    elif before is not None:
                        act.wait_ge(multiplied, (blk - 1) * NG + g - BUFS + NG + 1)
                    nc.scalar.activation(a_hi[:, g % BUFS, 0:n, :], turn_ps[g % BUFS][:, 0:n, :],
                                         ACT.Copy).then_inc(hi_made, 1)
                    if before == 0 and g == TURN_AT + 1:
                        act.wait_ge(x1_turned, blk)
                        nc.scalar.activation(x1T[0:D, :], epi[0:D, :], ACT.Copy).then_inc(x1T_made, 1)
                    if before == 0 and g == PROJECT_AT + 2:
                        act.wait_ge(hd_made, blk)
                        nc.scalar.activation(rhs1[:, bass.ds((blk - 1) * S, S), 0:D], hd[:],
                                             ACT.Copy).then_inc(rhs1_hi, 1)

            for i in range(PREP):
                piece = slice(i * PT, (i + 1) * PT)
                act.wait_ge(drop_made, 3 * (i + 1))
                nc.scalar.activation(rhs0[:, piece, 0:D - 1], drop[:, piece, 0:D - 1], ACT.Copy).then_inc(rhs0_hi, 1)
            blocks(act, body)
            evict(LAST)

        @block.vector
        def _(dve):
            def split_lo(blk, g):
                n = len(GROUPS[g])
                dve.wait_ge(hi_made, blk * NG + g + 1)
                nc.vector.tensor_tensor(a_lo[:, g % BUFS, 0:n, :], turn_ps[g % BUFS][:, 0:n, :],
                                        a_hi_f[:, g % BUFS, 0:n, :], ALU.subtract).then_inc(lo_made, 1)

            def residual(blk, layer):
                tiles = bass.ds((blk - layer * BLOCKS) * S, S)
                dve.wait_ge(folded, blk + 1)
                if layer == 0:
                    nc.vector.tensor_scalar(deg[:], z0[:, :, D], 1.0, None, ALU.add)
                    nc.vector.tensor_scalar(iszero[:], z0[:, :, D], 1.0, 0.0, ALU.add, ALU.is_equal)
                    nc.vector.tensor_scalar(nonzero[:], z0[:, :, D], 1.0, 0.0, ALU.add, ALU.not_equal)
                    nc.vector.tensor_tensor(pre[:], z0[:, :, 0:D], xt[:, tiles, :], ALU.add).then_inc(pre_made, 1)
                else:
                    nc.vector.tensor_tensor(pre[:], z1[:], rhs1_f[:, tiles, 0:D], ALU.add).then_inc(pre_made, 1)

            def relu_residual(blk):
                dve.wait_ge(scaled, blk - BLOCKS + 1)
                nc.vector.scalar_tensor_tensor(pre[:], pre[:], 0.0, xt[:, bass.ds((blk - BLOCKS) * S, S), :],
                                               ALU.max, ALU.add).then_inc(relu_made, 1)
                dve.wait_ge(relu_made, blk - BLOCKS + 1)

            def sums(blk, layer):
                if layer == 0:
                    dve.wait_ge(pre_made, blk + 1)
                else:
                    relu_residual(blk)
                nc.vector.tensor_reduce(rsum[:], pre[:], AX.X, ALU.add).then_inc(sums_made, 1)

            def square_sums(blk, layer):
                dve.wait_ge(cen_made, blk + 1)
                nc.vector.tensor_reduce(vsum[:], sq[:], AX.X, ALU.add).then_inc(vsums_made, 1)

            def scale_h(blk):
                dve.wait_ge(projected, blk + 1)
                dve.wait_ge(d_made, blk + 1)
                nc.vector.tensor_tensor(hd[:], z1[:], dnow[:].unsqueeze(2).to_broadcast([P, S, D]),
                                        ALU.mult).then_inc(hd_made, 1)

            def rhs1_lo_part(blk):
                tiles = bass.ds(blk * S, S)
                dve.wait_ge(rhs1_hi, blk + 1)
                nc.vector.tensor_tensor(rhs1[:, tiles, D:2 * D], hd[:], rhs1_f[:, tiles, 0:D],
                                        ALU.subtract).then_inc(rhs1_made, 1)

            def body(blk, layer, before):
                for g in range(NG):
                    split_lo(blk, g)
                    if before is None:
                        continue
                    if g == FOLD_AT + 1:
                        residual(blk - 1, before)
                        if before == 0:
                            sums(blk - 1, 0)
                    if before == 1 and g == FOLD_AT + 4:
                        sums(blk - 1, 1)
                    if g == FOLD_AT + 7:
                        square_sums(blk - 1, before)
                    if before == 0 and g == PROJECT_AT + 1:
                        scale_h(blk - 1)
                    if before == 0 and g == PROJECT_AT + 3:
                        rhs1_lo_part(blk - 1)

            nc.vector.memset(x1T[D:D + 1, :], 1.0).then_inc(ones_made, 1)
            nc.vector.memset(rhs0[:, :, D - 1:D].bitcast(fp32), 1.0)
            nc.vector.memset(rhs0[:, :, 2 * D - 1:2 * D].bitcast(fp32), 0.0)
            step = 0
            for i in range(PREP):
                piece = slice(i * PT, (i + 1) * PT)
                dve.wait_ge(x_in[i], 32)
                nc.vector.scalar_tensor_tensor(drop[:, piece, :], drop[:, piece, :], KEEP_FROM, xt[:, piece, :],
                                               ALU.is_ge, ALU.mult).then_inc(drop_made, 1)
                step += 1
                dve.wait_ge(drop_made, step)
                nc.vector.tensor_scalar(drop[:, piece, :], drop[:, piece, :], UNDROP, None,
                                        ALU.mult).then_inc(drop_made, 1)
                step += 1
                dve.wait_ge(drop_made, step)
                nc.vector.tensor_tensor(drop[:, piece, 0:D - 1], drop[:, piece, 0:D - 1],
                                        drop[:, piece, D - 1:D].to_broadcast([P, PT, D - 1]),
                                        ALU.subtract).then_inc(drop_made, 1)
                step += 1
                dve.wait_ge(rhs0_hi, i + 1)
                nc.vector.tensor_tensor(rhs0[:, piece, D:2 * D - 1], drop[:, piece, 0:D - 1],
                                        rhs0[:, piece, 0:D - 1].bitcast(fp32), ALU.subtract).then_inc(rhs0_lo, 1)
            blocks(dve, body)
            residual(LAST, 1)
            sums(LAST, 1)
            square_sums(LAST, 1)

        @block.gpsimd
        def _(pool):
            def diagonal(t, cols, off):
                return nc.gpsimd.affine_select(out=t[:, 0:cols], in_=t[:, 0:cols], compare_op=ALU.not_equal,
                                               fill=1.0, base=-off, pattern=[[-1, cols]], channel_multiplier=1)

            nc.gpsimd.memset(minus_half[:], -0.5)
            nc.gpsimd.memset(per_column[:], 1.0 / D)
            nc.gpsimd.memset(eps[:], EPS)
            nc.gpsimd.memset(ident[:], 0.0)
            nc.gpsimd.memset(fold0[:], 0.0)
            nc.gpsimd.memset(fold1[:], 0.0).then_inc(consts_made, 1)
            pool.wait_ge(consts_made, 1)
            diagonal(ident, P, 0)
            diagonal(fold0, D - 1, 0)
            diagonal(fold1, D, 0).then_inc(consts_made, 1)
            pool.wait_ge(consts_made, 2)
            diagonal(fold0, D - 1, D)
            diagonal(fold1, D, D)
            last_col = fold0[:, D:D + 1]
            nc.gpsimd.affine_select(out=last_col, in_=last_col, compare_op=ALU.not_equal, fill=1.0,
                                    base=-(D - 1), pattern=[[-1, 1]], channel_multiplier=1).then_inc(consts_made, 1)
            pool.wait_ge(consts_made, 3)
            nc.gpsimd.affine_select(out=last_col, in_=last_col, compare_op=ALU.not_equal, fill=1.0,
                                    base=-(2 * D - 1), pattern=[[-1, 1]], channel_multiplier=1).then_inc(consts_made, 1)

            def wide(t):
                return t[:].unsqueeze(2).to_broadcast([P, S, D])

            STEPS = (8, 6)

            def finish(blk, layer):
                i = blk - layer * BLOCKS
                tiles = bass.ds(i * S, S)
                base = i * STEPS[layer] + layer * BLOCKS * STEPS[0]
                done = [0]

                def step(ins):
                    ins.then_inc(pool_step, 1)
                    done[0] += 1
                    pool.wait_ge(pool_step, base + done[0])

                if layer == 1:
                    pool.wait_ge(pre_made, blk + 1)
                    nc.gpsimd.tensor_tensor(pre[:], pre[:], rhs1_f[:, tiles, D:2 * D], ALU.add)
                    step(nc.gpsimd.tensor_copy(dnow[:], d_all[:, tiles]))
                    nc.gpsimd.tensor_tensor(pre[:], pre[:], wide(dnow), ALU.mult).then_inc(scaled, 1)
                pool.wait_ge(sums_made, blk + 1)
                step(nc.gpsimd.tensor_tensor(mean[:], rsum[:], per_column[:], ALU.mult))
                step(nc.gpsimd.tensor_tensor(cen[:], pre[:], wide(mean), ALU.subtract))
                nc.gpsimd.tensor_tensor(sq[:], cen[:], cen[:], ALU.mult).then_inc(cen_made, 1)
                if layer == 0:
                    step(nc.gpsimd.tensor_tensor(degs[:], deg[:], iszero[:], ALU.add))
                    step(nc.gpsimd.tensor_tensor(dpow[:], degs[:], minus_half[:], ALU.pow))
                    step(nc.gpsimd.tensor_tensor(dnow[:], dpow[:], nonzero[:], ALU.mult))
                    nc.gpsimd.tensor_copy(d_all[:, tiles], dnow[:]).then_inc(d_made, 1)
                pool.wait_ge(vsums_made, blk + 1)
                step(nc.gpsimd.tensor_tensor(var[:], vsum[:], per_column[:], ALU.mult))
                step(nc.gpsimd.tensor_tensor(var[:], var[:], eps[:], ALU.add))
                step(nc.gpsimd.tensor_tensor(rstd[:], var[:], minus_half[:], ALU.pow))
                if layer == 1 and not (isinstance(blk, int) and blk == BLOCKS):
                    pool.wait_ge(out_stored, 16 * (blk - BLOCKS))
                nc.gpsimd.tensor_tensor(normed[:], cen[:], wide(rstd), ALU.mult).then_inc(normed_made, 1)
                if layer == 0:
                    pool.wait_ge(normed_made, blk + 1)
                    nc.gpsimd.tensor_copy(xt[:, tiles, :], normed[:]).then_inc(x1_kept, 1)

            with pool.Fori(0, BLOCKS) as i:
                finish(i, 0)
            finish(BLOCKS, 1)
            with pool.Fori(BLOCKS + 1, LAST + 1) as i:
                finish(i, 1)


_INS = ['x', 'adj', 'L0_gnn_u', 'L1_gnn_W', 'L1_gnn_b']


def kernel(**inputs):
    import numpy as _np
    import concourse.bacc as _bacc
    from concourse import mybir as _mybir
    from concourse.bass_utils import run_bass_kernel_spmd as _run

    nc = _bacc.Bacc("TRN2", target_bir_lowering=False, num_devices=1)
    arrays, args = {}, []
    for name in _INS:
        a = _np.ascontiguousarray(inputs[name])
        arrays[f"in_{name}_dram"] = a
        args.append(nc.dram_tensor(f"in_{name}_dram", a.shape, _mybir.dt.from_np(a.dtype), kind="ExternalInput").ap())
    shape = inputs['x'].shape
    out = nc.dram_tensor("out_0_dram", shape, _mybir.dt.float32, kind="ExternalOutput").ap()
    two_layer_graph_resnorm(nc, *args, out)
    r = _run(nc, [arrays], core_ids=[0])
    return r.results[0]["out_0_dram"]
```

```python
import concourse.bass as bass
from concourse import mybir
from contextlib import ExitStack
import numpy as np

P = 128
ROWS = 512
HELD = 2
EARLY = 9
EARLY_CHUNKS = 5


def visit_order(blocks):
    order, second = [], {r: list(range(r + HELD + 1, blocks)) for r in range(blocks)}

    def again(r, c):
        second[r].remove(c)
        order.append((r, c, (1,), True))

    def from_hold(c):
        for r in range(max(0, c - HELD), c + 1):
            order.append((r, c, (1,), False))

    for b in range(blocks):
        mine = [(b, c, (0,), True) for c in range(b + HELD + 1, blocks)]
        mine += [(b, c, (0, 1), True) for c in range(b)]
        mine += [(b, c, (0,), True) for c in range(b, min(b + HELD + 1, blocks))]
        if b >= EARLY:
            for c in second[b - EARLY][:EARLY_CHUNKS]:
                again(b - EARLY, c)
        order += mine[:11]
        if b:
            from_hold(b - 1)
        order += mine[11:]
    for r in (0, 7):
        for c in second[r][:-1]:
            again(r, c)
    from_hold(blocks - 1)
    for r in (0, 7, 1, 12, 2, 11, 3, 10, 6, 4, 9, 5, 8):
        for c in list(second[r]):
            again(r, c)
    assert not any(second.values())
    return order


def two_layer_graph_resnorm(nc, x, adj, u, w, b, out):
    fp32 = mybir.dt.float32
    fp32r = mybir.dt.float32r
    ALU = mybir.AluOpType
    ACT = mybir.ActivationFunctionType
    AX = mybir.AxisListType

    KT, D = x.shape[1], x.shape[2]
    KEEP_FROM = 0.1
    UNDROP = float(np.float32(1.0) / np.float32(0.9))
    EPS = 1e-5

    BLOCKS = KT * P // ROWS
    S = ROWS // P
    PAIRS = S // 2
    SLOTS = 9
    BUFS = 3
    ACC1 = 5
    PREP = 8
    PT = KT // PREP
    PIECES = list(range(1, PREP)) + [0]
    U_SLOT = SLOTS - 2

    VISITS = visit_order(BLOCKS)
    LOADS = [v for v, visit in enumerate(VISITS) if visit[3]]

    last_visit = {}
    for v, (r, c, _, loaded) in enumerate(VISITS):
        if loaded:
            held_by = v
        else:
            held_by = max(n for n in LOADS if n < v and VISITS[n][:2] == (r, c))
        last_visit[held_by] = v
    slot_of, free_after, load_count, uses = {}, {}, {}, [-1] * SLOTS
    loads_into = [0] * SLOTS
    for v in LOADS:
        slot = min(range(SLOTS), key=lambda i: (uses[i], i))
        assert uses[slot] < v
        free_after[v] = uses[slot]
        uses[slot] = last_visit[v]
        loads_into[slot] += 1
        slot_of[v] = (slot, loads_into[slot])
    for v, (r, c, _, loaded) in enumerate(VISITS):
        if not loaded:
            slot_of[v] = slot_of[max(n for n in LOADS if n < v and VISITS[n][:2] == (r, c))]

    def product_of(v, layer):
        r, c = VISITS[v][0:2]
        if layer == 0:
            return 0, r, 0
        if not VISITS[v][3] or c < r:
            return 1, r, 0
        return 1, r, 1 if v < early_end else 2

    early_end = max(v for v, visit in enumerate(VISITS) if 0 in visit[2]) + 1
    first_visit, final_visit = {}, {}
    for v, visit in enumerate(VISITS):
        for layer in visit[2]:
            g = product_of(v, layer)
            first_visit.setdefault(g, v)
            final_visit[g] = v
    PRODUCTS = sorted(final_visit, key=lambda g: (final_visit[g], g))
    ENDS = [final_visit[g] * PAIRS + PAIRS - 1 for g in PRODUCTS]
    bank_of, bank_before, held_until = {}, {}, [(-1, None)] * ACC1
    for g in sorted((g for g in PRODUCTS if g[0] == 1), key=lambda g: first_visit[g]):
        i = min(range(ACC1), key=lambda i: held_until[i][0])
        assert held_until[i][0] < first_visit[g]
        bank_of[g], bank_before[g] = i, held_until[i][1]
        held_until[i] = (final_visit[g], g)

    steps = [[] for _ in range(len(VISITS) * PAIRS + 40)]

    def beside(pair, name, arg):
        steps[pair].append((name, arg))

    NORMS = []
    norm_at = []
    rhs1_at = {}
    for j, g in enumerate(PRODUCTS):
        e = ENDS[j]
        beside(e + 3, "evict", j)
        beside(e + 4, "fold", j)
        beside(e + 6, "absorb", j)
        last_of_row = g[0] == 1 and all(ENDS[i] < e or i == j for i, h in enumerate(PRODUCTS) if h[:2] == g[:2]
                                        ) and not any(h[:2] == g[:2] for h in PRODUCTS[j + 1:])
        if g[0] == 1 and not last_of_row:
            continue
        q = len(NORMS)
        t = e + (6 if g[0] == 0 else 8)
        if q:
            t = max(t, norm_at[-1] + 3)
        NORMS.append(g[:2])
        norm_at.append(t)
        if g[0] == 1:
            beside(t - 1, "scale", q)
        beside(t, "sums", q)
        beside(t + 1, "centre", q)
        beside(t + 3, "squares", q)
        beside(t + 4, "normalise", q)
        if g[0] == 0:
            beside(t + 6, "turn x1", q)
            beside(t + 7, "keep x1T", q)
            beside(t + 8, "project", q)
            beside(t + 10, "scale h", q)
            beside(t + 11, "rhs1 hi", q)
            beside(t + 12, "rhs1 lo", q)
            rhs1_at[g[1]] = t + 12
    assert NORMS[:BLOCKS] == [(0, r) for r in range(BLOCKS)] and len(NORMS) == 2 * BLOCKS
    for v, (r, c, layers, _) in enumerate(VISITS):
        assert 1 not in layers or v * PAIRS > rhs1_at[c]
    NSETS = 2

    ctx = ExitStack()
    with ctx:
        def sb(name, shape, dt=fp32):
            return ctx.enter_context(nc.sbuf_tensor(name, shape, dt))

        def ps(name, shape, dt=fp32):
            return ctx.enter_context(nc.psum_tensor(name, shape, dt))

        def sem(name):
            return ctx.enter_context(nc.semaphore(name))

        ring = sb("adj_ring", [P, SLOTS, S * ROWS])
        drop = ring[:, U_SLOT:U_SLOT + 2, :].rearrange("p s (t d) -> p (s t) d", d=D)
        rhs0 = sb("rhs_layer0", [P, KT, 2 * D], fp32r)
        rhs1 = sb("rhs_layer1", [P, KT, 2 * D], fp32r)
        rhs1_f = rhs1[:].bitcast(fp32)
        xt = sb("x_table", [P, KT, D])
        sum1 = sb("sum_layer1", [P, KT, D])
        a_hi = sb("adj_hi", [P, BUFS, 2, ROWS], fp32r)
        a_hi_f = a_hi[:].bitcast(fp32)
        a_lo = sb("adj_lo", [P, BUFS, 2, ROWS], fp32r)
        acc_sb = sb("acc_sb", [P, ROWS])
        ident = sb("ident", [P, P])
        fold0 = sb("fold0", [P, D + 1])
        fold1 = sb("fold1", [P, D])
        wb = sb("w_and_b", [D + 1, D])
        pre, cen = (sb(n, [P, NSETS, S, D]) for n in ("pre_norm", "centred"))
        sq = sb("squared", [P, S, D])
        normed = sb("normed", [P, NSETS, S, D])
        x1T = sb("x1_turned", [D + 1, ROWS])
        d_all = sb("d_table", [P, KT])
        rsum, vsum = (sb(n, [P, NSETS, S]) for n in ("rsum", "vsum"))
        mean, var, rstd, deg, iszero, degs, dpow, nonzero = (
            sb(n, [P, S]) for n in ("mean", "var", "rstd", "deg", "iszero", "degs", "dpow", "nonzero"))
        minus_half, per_column, eps = (sb(n, [P, S]) for n in ("minus_half", "per_column", "eps"))

        acc0 = ps("acc0", [P, ROWS])
        acc1 = [ps(f"acc1_{i}", [P, ROWS]) for i in range(ACC1)]
        folded_ps = ps("folded_ps", [P, ROWS])
        h_ps = ps("h_ps", [P, ROWS])
        z0 = folded_ps[:, 0:S * (D + 1)].rearrange("p (s d) -> p s d", s=S)
        z1 = folded_ps[:, 0:S * D].rearrange("p (s d) -> p s d", s=S)
        h = h_ps[:, 0:S * D].rearrange("p (s d) -> p s d", s=S)

        x_in = [sem(f"x_in{i}") for i in range(PREP)]
        u_in = [sem(f"u_in{i}") for i in range(PREP)]
        w_in = sem("w_in")
        adj_in = [sem(f"adj_in{i}") for i in range(SLOTS)]
        out_stored = [sem(f"out_stored{i}") for i in range(NSETS)]
        consts_made = sem("consts_made")
        ones_made = sem("ones_made")
        kept = sem("kept")
        shifted = sem("shifted")
        rhs0_hi = sem("rhs0_hi")
        rhs0_made = sem("rhs0_made")
        hi_made = sem("hi_made")
        lo_made = sem("lo_made")
        multiplied = sem("multiplied")
        evicted = sem("evicted")
        folded = sem("folded")
        absorbed = sem("absorbed")
        scaled = sem("scaled")
        relu_made = sem("relu_made")
        sums_made = sem("sums_made")
        cen_made = sem("cen_made")
        squared = sem("squared_made")
        vsums_made = sem("vsums_made")
        normed_made = sem("normed_made")
        d_made = sem("d_made")
        x1_turned = sem("x1_turned_made")
        x1T_made = sem("x1T_made")
        projected = sem("projected")
        hd_made = sem("hd_made")
        rhs1_hi = sem("rhs1_hi")
        rhs1_made = sem("rhs1_made")
        pool_step = sem("pool_step")

        def tiles_of(r):
            return slice(r * S, (r + 1) * S)

        block = ctx.enter_context(nc.Block())

        @block.sync
        def _(sp):
            def load_piece(i):
                piece = slice(i * PT, (i + 1) * PT)
                sp.dma_start(drop[:, piece, :], u[:, piece, :]).then_inc(u_in[i], 16)
                sp.dma_start(xt[:, piece, :], x[:, piece, :]).then_inc(x_in[i], 16)

            pieces = list(PIECES)
            load_piece(pieces.pop(0))
            for n, v in enumerate(LOADS):
                slot, _ = slot_of[v]
                if n >= U_SLOT and n < SLOTS:
                    sp.wait_ge(rhs0_made, PREP)
                if free_after[v] >= 0:
                    sp.wait_ge(lo_made, (free_after[v] + 1) * PAIRS)
                sp.dma_start(ring[:, slot, :], adj[VISITS[v][0], VISITS[v][1]]).then_inc(adj_in[slot], 16)
                if pieces:
                    load_piece(pieces.pop(0))
                if pieces and n:
                    load_piece(pieces.pop(0))
                if n == 2:
                    sp.dma_start(wb[0:D, :], w).then_inc(w_in, 16)
                    sp.dma_start(wb[D:D + 1, :], b.rearrange("(o d) -> o d", o=1)).then_inc(w_in, 16)

        @block.tensor
        def _(pe):
            def multiply(n, seen):
                v, half = divmod(n, PAIRS)
                r, c, layers, _ = VISITS[v]
                if half == 0:
                    piece = PIECES.index(c * S // PT) + 1
                    if 0 in layers and piece > seen["rhs0"]:
                        pe.wait_ge(rhs0_made, piece)
                        seen["rhs0"] = piece
                    if 1 in layers and c + 1 > seen["rhs1"]:
                        pe.wait_ge(rhs1_made, c + 1)
                        seen["rhs1"] = c + 1
                    for layer in layers:
                        g = product_of(v, layer)
                        before = ((0, r - 1, 0) if r else None) if layer == 0 else bank_before[g]
                        if first_visit[g] == v and before:
                            pe.wait_ge(evicted, PRODUCTS.index(before) + 1)
                pe.wait_ge(lo_made, n + 1)
                for i in range(2):
                    k = c * S + half * 2 + i
                    for layer in layers:
                        g = product_of(v, layer)
                        rhs, to = (rhs1, acc1[bank_of[g]]) if layer else (rhs0, acc0)
                        for part in (a_hi, a_lo):
                            last = nc.tensor.matmul(
                                to[:], rhs[:, k, :], part[:, n % BUFS, i, :],
                                start=(v == first_visit[g] and half == 0 and i == 0 and part is a_hi),
                                stop=(v == final_visit[g] and half == PAIRS - 1 and i == 1 and part is a_lo))
                last.then_inc(multiplied, 1)

            def fold(j):
                f, width = (fold1, D) if PRODUCTS[j][0] else (fold0, D + 1)
                pe.wait_ge(evicted, j + 1)
                if j:
                    pe.wait_ge(absorbed, j)
                for s in range(S):
                    last = nc.tensor.matmul(folded_ps[:, s * width:(s + 1) * width], acc_sb[:, s * P:(s + 1) * P],
                                            f[:], start=True, stop=True)
                last.then_inc(folded, 1)

            def turn_x1(q):
                pe.wait_ge(normed_made, q + 1)
                if q:
                    pe.wait_ge(hd_made, q)
                for s in range(S):
                    last = nc.tensor.transpose(h_ps[0:D, s * P:(s + 1) * P], normed[:, q % NSETS, s, :], ident[:])
                last.then_inc(x1_turned, 1)

            def project(q):
                pe.wait_ge(x1T_made, q + 1)
                for s in range(S):
                    last = nc.tensor.matmul(h_ps[:, s * D:(s + 1) * D], x1T[:, s * P:(s + 1) * P], wb[:],
                                            start=True, stop=True)
                last.then_inc(projected, 1)

            pe.wait_ge(consts_made, 4)
            pe.wait_ge(ones_made, 1)
            pe.wait_ge(w_in, 32)
            seen = {"rhs0": 0, "rhs1": 0}
            for n, beside_n in enumerate(steps):
                if n < len(VISITS) * PAIRS:
                    multiply(n, seen)
                for name, arg in beside_n:
                    if name == "fold":
                        fold(arg)
                    elif name == "turn x1":
                        turn_x1(arg)
                    elif name == "project":
                        project(arg)

        @block.scalar
        def _(act):
            def split_hi(n):
                v, half = divmod(n, PAIRS)
                slot, count = slot_of[v]
                if half == 0:
                    act.wait_ge(adj_in[slot], 16 * count)
                if n >= BUFS:
                    act.wait_ge(multiplied, n - BUFS + 1)
                nc.scalar.activation(a_hi[:, n % BUFS, :, :],
                                     ring[:, slot, half * 2 * ROWS:(half + 1) * 2 * ROWS], ACT.Copy).then_inc(hi_made, 1)

            def evict(j):
                g = PRODUCTS[j]
                act.wait_ge(multiplied, ENDS[j] + 1)
                if j:
                    act.wait_ge(folded, j)
                nc.scalar.activation(acc_sb[:], (acc1[bank_of[g]] if g[0] else acc0)[:], ACT.Copy).then_inc(evicted, 1)

            def keep_x1T(q):
                act.wait_ge(x1_turned, q + 1)
                nc.scalar.activation(x1T[0:D, :], h_ps[0:D, :], ACT.Copy).then_inc(x1T_made, 1)

            def rhs1_hi_part(q):
                act.wait_ge(hd_made, q + 1)
                nc.scalar.activation(rhs1[:, tiles_of(q), 0:D], sum1[:, tiles_of(q), :], ACT.Copy).then_inc(rhs1_hi, 1)

            for i, piece in enumerate(PIECES):
                tiles = slice(piece * PT, (piece + 1) * PT)
                act.wait_ge(shifted, i + 1)
                nc.scalar.activation(rhs0[:, tiles, 0:D - 1], drop[:, tiles, 0:D - 1], ACT.Copy).then_inc(rhs0_hi, 1)
            for n, beside_n in enumerate(steps):
                for name, arg in beside_n:
                    if name == "evict":
                        evict(arg)
                    elif name == "keep x1T":
                        keep_x1T(arg)
                    elif name == "rhs1 hi":
                        rhs1_hi_part(arg)
                if n < len(VISITS) * PAIRS:
                    split_hi(n)

        @block.vector
        def _(dve):
            def split_lo(n):
                v, half = divmod(n, PAIRS)
                slot, _ = slot_of[v]
                dve.wait_ge(hi_made, n + 1)
                nc.vector.tensor_tensor(a_lo[:, n % BUFS, :, :],
                                        ring[:, slot, half * 2 * ROWS:(half + 1) * 2 * ROWS].rearrange(
                                            "p (k i) -> p k i", k=2),
                                        a_hi_f[:, n % BUFS, :, :], ALU.subtract).then_inc(lo_made, 1)

            def absorb(j):
                layer, r, _ = PRODUCTS[j]
                dve.wait_ge(folded, j + 1)
                if layer == 0:
                    if r:
                        dve.wait_ge(d_made, r)
                    nc.vector.tensor_scalar(deg[:], z0[:, :, D], 1.0, None, ALU.add)
                    nc.vector.tensor_scalar(iszero[:], z0[:, :, D], 1.0, 0.0, ALU.add, ALU.is_equal)
                    nc.vector.tensor_scalar(nonzero[:], z0[:, :, D], 1.0, 0.0, ALU.add, ALU.not_equal)
                    if r >= NSETS:
                        dve.wait_ge(cen_made, r - NSETS + 1)
                    nc.vector.tensor_tensor(pre[:, r % NSETS], z0[:, :, 0:D], xt[:, tiles_of(r), :],
                                            ALU.add).then_inc(absorbed, 1)
                else:
                    nc.vector.tensor_tensor(sum1[:, tiles_of(r), :], z1[:], sum1[:, tiles_of(r), :],
                                            ALU.add).then_inc(absorbed, 1)

            def sums(q):
                layer, r = NORMS[q]
                if layer == 0:
                    dve.wait_ge(absorbed, PRODUCTS.index((0, r, 0)) + 1)
                else:
                    dve.wait_ge(scaled, q - BLOCKS + 1)
                    nc.vector.scalar_tensor_tensor(pre[:, q % NSETS], pre[:, q % NSETS], 0.0, xt[:, tiles_of(r), :],
                                                   ALU.max, ALU.add).then_inc(relu_made, 1)
                    dve.wait_ge(relu_made, q - BLOCKS + 1)
                if q >= NSETS:
                    dve.wait_ge(cen_made, q - NSETS + 1)
                nc.vector.tensor_reduce(rsum[:, q % NSETS], pre[:, q % NSETS], AX.X, ALU.add).then_inc(sums_made, 1)

            def square_sums(q):
                dve.wait_ge(squared, q + 1)
                nc.vector.tensor_reduce(vsum[:, q % NSETS], sq[:], AX.X, ALU.add).then_inc(vsums_made, 1)

            def scale_h(q):
                dve.wait_ge(projected, q + 1)
                dve.wait_ge(d_made, q + 1)
                nc.vector.tensor_tensor(sum1[:, tiles_of(q), :], h[:],
                                        d_all[:, tiles_of(q)].unsqueeze(2).to_broadcast([P, S, D]),
                                        ALU.mult).then_inc(hd_made, 1)

            def rhs1_lo_part(q):
                dve.wait_ge(rhs1_hi, q + 1)
                nc.vector.tensor_tensor(rhs1[:, tiles_of(q), D:2 * D], sum1[:, tiles_of(q), :],
                                        rhs1_f[:, tiles_of(q), 0:D], ALU.subtract).then_inc(rhs1_made, 1)

            nc.vector.memset(x1T[D:D + 1, :], 1.0).then_inc(ones_made, 1)
            nc.vector.memset(rhs0[:, :, D - 1:D].bitcast(fp32), 1.0)
            nc.vector.memset(rhs0[:, :, 2 * D - 1:2 * D].bitcast(fp32), 0.0)
            for i, piece in enumerate(PIECES):
                tiles = slice(piece * PT, (piece + 1) * PT)
                dve.wait_ge(kept, 2 * (i + 1))
                nc.vector.tensor_tensor(drop[:, tiles, 0:D - 1], drop[:, tiles, 0:D - 1],
                                        drop[:, tiles, D - 1:D].to_broadcast([P, PT, D - 1]),
                                        ALU.subtract).then_inc(shifted, 1)
                dve.wait_ge(rhs0_hi, i + 1)
                nc.vector.tensor_tensor(rhs0[:, tiles, D:2 * D - 1], drop[:, tiles, 0:D - 1],
                                        rhs0[:, tiles, 0:D - 1].bitcast(fp32), ALU.subtract).then_inc(rhs0_made, 1)
            for n, beside_n in enumerate(steps):
                if n < len(VISITS) * PAIRS:
                    split_lo(n)
                for name, arg in beside_n:
                    if name == "absorb":
                        absorb(arg)
                    elif name == "sums":
                        sums(arg)
                    elif name == "squares":
                        square_sums(arg)
                    elif name == "scale h":
                        scale_h(arg)
                    elif name == "rhs1 lo":
                        rhs1_lo_part(arg)

        @block.gpsimd
        def _(pool):
            def diagonal(t, cols, off):
                return nc.gpsimd.affine_select(out=t[:, 0:cols], in_=t[:, 0:cols], compare_op=ALU.not_equal,
                                               fill=1.0, base=-off, pattern=[[-1, cols]], channel_multiplier=1)

            for i, piece in enumerate(PIECES):
                tiles = slice(piece * PT, (piece + 1) * PT)
                pool.wait_ge(u_in[piece], 16)
                nc.gpsimd.tensor_scalar(drop[:, tiles, :], drop[:, tiles, :], KEEP_FROM, UNDROP,
                                        ALU.is_ge, ALU.mult).then_inc(kept, 1)
                pool.wait_ge(x_in[piece], 16)
                pool.wait_ge(kept, 2 * i + 1)
                nc.gpsimd.tensor_tensor(drop[:, tiles, :], drop[:, tiles, :], xt[:, tiles, :],
                                        ALU.mult).then_inc(kept, 1)
                if i:
                    continue
                nc.gpsimd.memset(minus_half[:], -0.5)
                nc.gpsimd.memset(per_column[:], 1.0 / D)
                nc.gpsimd.memset(eps[:], EPS)
                nc.gpsimd.memset(ident[:], 0.0)
                nc.gpsimd.memset(fold0[:], 0.0)
                nc.gpsimd.memset(fold1[:], 0.0).then_inc(consts_made, 1)
                pool.wait_ge(consts_made, 1)
                diagonal(ident, P, 0)
                diagonal(fold0, D - 1, 0)
                diagonal(fold1, D, 0).then_inc(consts_made, 1)
                pool.wait_ge(consts_made, 2)
                diagonal(fold0, D - 1, D)
                diagonal(fold1, D, D)
                ones = fold0[:, D:D + 1]
                nc.gpsimd.affine_select(out=ones, in_=ones, compare_op=ALU.not_equal, fill=1.0, base=-(D - 1),
                                        pattern=[[-1, 1]], channel_multiplier=1).then_inc(consts_made, 1)
                pool.wait_ge(consts_made, 3)
                nc.gpsimd.affine_select(out=ones, in_=ones, compare_op=ALU.not_equal, fill=1.0, base=-(2 * D - 1),
                                        pattern=[[-1, 1]], channel_multiplier=1).then_inc(consts_made, 1)

            def wide(t):
                return t.unsqueeze(2).to_broadcast([P, S, D])

            done = [0]

            def step(ins):
                ins.then_inc(pool_step, 1)
                done[0] += 1
                pool.wait_ge(pool_step, done[0])

            def scale(q):
                r = NORMS[q][1]
                pool.wait_ge(absorbed, max(j for j, g in enumerate(PRODUCTS) if g[:2] == (1, r)) + 1)
                nc.gpsimd.tensor_tensor(pre[:, q % NSETS], sum1[:, tiles_of(r), :], wide(d_all[:, tiles_of(r)]),
                                        ALU.mult).then_inc(scaled, 1)

            def centre(q):
                layer, r = NORMS[q]
                i = q % NSETS
                pool.wait_ge(sums_made, q + 1)
                step(nc.gpsimd.tensor_tensor(mean[:], rsum[:, i], per_column[:], ALU.mult))
                nc.gpsimd.tensor_tensor(cen[:, i], pre[:, i], wide(mean[:]), ALU.subtract).then_inc(cen_made, 1)
                pool.wait_ge(cen_made, q + 1)
                if q:
                    pool.wait_ge(vsums_made, q)
                nc.gpsimd.tensor_tensor(sq[:], cen[:, i], cen[:, i], ALU.mult).then_inc(squared, 1)
                if layer == 0:
                    step(nc.gpsimd.tensor_tensor(degs[:], deg[:], iszero[:], ALU.add))
                    step(nc.gpsimd.tensor_tensor(dpow[:], degs[:], minus_half[:], ALU.pow))
                    nc.gpsimd.tensor_tensor(d_all[:, tiles_of(r)], dpow[:], nonzero[:], ALU.mult).then_inc(d_made, 1)

            def normalise(q):
                layer, r = NORMS[q]
                i = q % NSETS
                pool.wait_ge(vsums_made, q + 1)
                step(nc.gpsimd.tensor_tensor(var[:], vsum[:, i], per_column[:], ALU.mult))
                step(nc.gpsimd.tensor_tensor(var[:], var[:], eps[:], ALU.add))
                step(nc.gpsimd.tensor_tensor(rstd[:], var[:], minus_half[:], ALU.pow))
                if layer == 0 and q >= NSETS:
                    pool.wait_ge(x1_turned, q - NSETS + 1)
                if layer == 1 and q >= BLOCKS + NSETS:
                    pool.wait_ge(out_stored[i], 16 * ((q - BLOCKS) // NSETS))
                if layer == 1 and q < BLOCKS + NSETS:
                    pool.wait_ge(x1_turned, BLOCKS)
                nc.gpsimd.tensor_tensor(normed[:, i], cen[:, i], wide(rstd[:]), ALU.mult).then_inc(normed_made, 1)
                pool.wait_ge(normed_made, q + 1)
                if layer == 0:
                    nc.gpsimd.tensor_copy(xt[:, tiles_of(r), :], normed[:, i])
                else:
                    pool.dma_start(out[:, tiles_of(r), :], normed[:, i]).then_inc(out_stored[i], 16)

            for beside_n in steps:
                for name, arg in beside_n:
                    if name == "scale":
                        scale(arg)
                    elif name == "centre":
                        centre(arg)
                    elif name == "normalise":
                        normalise(arg)
            for i in range(NSETS):
                pool.wait_ge(out_stored[i], 16 * (BLOCKS // NSETS))


_INS = ['x', 'adj', 'L0_gnn_u', 'L1_gnn_W', 'L1_gnn_b']


def kernel(**inputs):
    import numpy as _np
    import concourse.bacc as _bacc
    from concourse import mybir as _mybir
    from concourse.bass_utils import run_bass_kernel_spmd as _run

    n, d = inputs['x'].shape
    t = n // P

    def laid_out(name):
        a = _np.asarray(inputs[name])
        if name == 'adj':
            a = a.reshape(n // ROWS, ROWS, n // ROWS, ROWS // P, P).transpose(0, 2, 4, 3, 1)
            a = a.reshape(n // ROWS, n // ROWS, P, ROWS * ROWS // P)
        elif name in ('x', 'L0_gnn_u'):
            a = a.reshape(t, P, d).transpose(1, 0, 2)
        return _np.ascontiguousarray(a)

    nc = _bacc.Bacc("TRN2", target_bir_lowering=False, num_devices=1)
    arrays, args = {}, []
    for name in _INS:
        a = laid_out(name)
        arrays[f"in_{name}_dram"] = a
        args.append(nc.dram_tensor(f"in_{name}_dram", a.shape, _mybir.dt.from_np(a.dtype), kind="ExternalInput").ap())
    out = nc.dram_tensor("out_0_dram", (P, t, d), _mybir.dt.float32, kind="ExternalOutput").ap()
    two_layer_graph_resnorm(nc, *args, out)
    r = _run(nc, [arrays], core_ids=[0])
    got = _np.asarray(r.results[0]["out_0_dram"])
    return _np.ascontiguousarray(got.transpose(1, 0, 2)).reshape(n, d)
```

```python
import concourse.bass as bass
from concourse import mybir
from contextlib import ExitStack
import numpy as np

P = 128
ROWS = 512
SLOTS = 9
BUFS = 4

HELD = [3, 2, 2, 3, 2, 2, 2, 2, 2, 2, 2, 2, 2, 2, 1, 1]
SECOND_VISITS = [0, 0, 0, 1, 0, 7, 0, 0, 0, 0, 0, 0, 4, 12, 12, 7]
READY = [15, 14, 13, 15, 15, 15, 15, 15, 16, 16, 16, 16, 16, 16, 16, 15, 15]

AFTER = dict(
    evict=4,
    fold=0,
    absorb=3,
    sums0=0,
    sums1=1,
    centre=0,
    squares=2,
    normalise=5,
    turn=4,
    keep=5,
    turn_last=5,
    keep_last=5,
    project=0,
    scale_h=3,
    rhs1_hi=3,
    rhs1_lo=0,
)
FOLD_GAP = 4
NORM_GAP = (5, 5)
STORE_LAG = 9
RHS0_LEAD = 9
PIECE_LEAD = 2


def visit_order(blocks):
    order, second = [], {r: list(range(r + HELD[r] + 1, blocks)) for r in range(blocks)}

    def again(r, c):
        second[r].remove(c)
        return r, c, (1,), True

    def from_hold(c):
        return [(r, c, (1,), False) for r in range(c + 1) if c <= r + HELD[r]]

    for b in range(blocks):
        only0 = [(b, c, (0,), True) for c in range(b + HELD[b] + 1, blocks)]
        both = [(b, c, (0, 1), True) for c in range(b)]
        keep = [(b, c, (0,), True) for c in range(b, min(b + HELD[b] + 1, blocks))]
        held = from_hold(b - 1) if b else []
        for _ in range(SECOND_VISITS[b]):
            r = min((r for r in range(b) if second[r] and second[r][0] < b - 1), default=None)
            if r is not None:
                only0.append(again(r, second[r][0]))
        n = len(only0) + len(both) + len(keep) + len(held)
        placed = []

        def spread(visits, first, end):
            for i, visit in enumerate(visits):
                placed.append((first + (end - first) * (i + 0.5) / len(visits), visit))

        spread(both[:-1], 0, n - 1)
        spread(only0, 0, n - len(keep))
        spread(held + both[-1:], min(READY[b], n - 3), n)
        spread(keep, n - 2 * len(keep), n)
        order += [visit for _, visit in sorted(placed, key=lambda at: at[0])]
    tail = 0
    for r in sorted((r for r in range(blocks) if second[r]), key=lambda r: len(second[r]))[::-1]:
        if tail < READY[blocks]:
            early = [again(r, c) for c in list(second[r]) if c < blocks - 1]
            tail += len(early)
            order += early
    rows = [[again(r, c) for c in list(second[r])] for r in sorted(second, key=lambda r: (len(second[r]), r)) if second[r]]
    rows += [[visit] for visit in from_hold(blocks - 1)]
    rows.sort(key=len)
    last = []
    while rows:
        short = rows.pop(0)
        last = short + (rows.pop() if rows else []) + last
    order += last
    assert not any(second.values())
    return order


def two_layer_graph_resnorm(nc, x, adj, u, w, b, out):
    fp32 = mybir.dt.float32
    fp32r = mybir.dt.float32r
    ALU = mybir.AluOpType
    ACT = mybir.ActivationFunctionType
    AX = mybir.AxisListType

    KT, D = x.shape[1], x.shape[2]
    KEEP_FROM = 0.1
    UNDROP = float(np.float32(1.0) / np.float32(0.9))
    EPS = 1e-5

    BLOCKS = KT * P // ROWS
    S = ROWS // P
    PAIRS = S // 2
    ACCS = 6
    PREP = 8
    PT = KT // PREP
    PIECES = list(range(1, PREP)) + [0]
    PIECE_PAIRS = PT // S * PAIRS
    U_SLOT = SLOTS - 2
    U_VISIT = (PIECE_PAIRS * (PREP - 1) - RHS0_LEAD + 3) // PAIRS

    VISITS = visit_order(BLOCKS)
    LOADS = [v for v, visit in enumerate(VISITS) if visit[3]]

    def product_of(v, layer):
        r, c = VISITS[v][0:2]
        if layer == 0:
            return 0, r, 0
        if not VISITS[v][3] or c < r:
            return 1, r, 0
        return 1, r, part_of[v]

    part_of, parts, last_row = {}, [0] * BLOCKS, None
    for v, (r, c, layers, loaded) in enumerate(VISITS):
        if loaded and c >= r and 1 in layers:
            if r != last_row:
                parts[r] += 1
            last_row = r
            part_of[v] = parts[r]
    first_visit, final_visit = {}, {}
    for v, visit in enumerate(VISITS):
        for layer in visit[2]:
            g = product_of(v, layer)
            first_visit.setdefault(g, v)
            final_visit[g] = v
    PRODUCTS = sorted(final_visit, key=lambda g: (final_visit[g], g))
    ENDS = [final_visit[g] * PAIRS + PAIRS - 1 for g in PRODUCTS]
    bank_of, bank_before, held_until = {}, {}, [(-1, None)] * ACCS
    for g in sorted(PRODUCTS, key=lambda g: first_visit[g]):
        i = min(range(ACCS), key=lambda i: held_until[i][0])
        assert held_until[i][0] < first_visit[g], "banks"
        bank_of[g], bank_before[g] = i, held_until[i][1]
        held_until[i] = (final_visit[g], g)

    steps = [[] for _ in range(len(VISITS) * PAIRS + 60)]

    def beside(pair, name, arg):
        steps[pair].append((name, arg))

    for i in range(PREP):
        at = max(1, PIECE_PAIRS * i - RHS0_LEAD) if i > 1 else 0
        beside(at, "mask x", i)
        beside(at + (1 if i > 1 else 0), "split rhs0", i)

    NORMS = []
    fold_at, absorb_at, norm_at, scale_h_at, rhs1_at = [], [], [], [], []
    for j, g in enumerate(PRODUCTS):
        t = ENDS[j] + AFTER["evict"]
        if j:
            t = max(t, fold_at[-1] + FOLD_GAP)
        beside(t, "evict", j)
        t += AFTER["fold"]
        if j:
            t = max(t, absorb_at[-1])
        beside(t, "fold", j)
        fold_at.append(t)
        t += AFTER["absorb"]
        beside(t, "absorb", j)
        absorb_at.append(t)
        if g[0] == 1 and any(later[:2] == g[:2] for later in PRODUCTS[j + 1:]):
            continue
        q = len(NORMS)
        NORMS.append(g[:2])
        t += AFTER["sums1"] if g[0] else AFTER["sums0"]
        if q:
            t = max(t, norm_at[-1] + NORM_GAP[g[0]])
        norm_at.append(t)
        if g[0] == 1:
            beside(t - 1, "scale", q)
        beside(t, "sums", q)
        beside(t + AFTER["centre"], "centre", q)
        beside(t + AFTER["squares"], "squares", q)
        beside(t + AFTER["normalise"], "normalise", q)
        if g[0] == 0:
            last = "_last" if q == BLOCKS - 1 else ""
            t += AFTER["turn" + last]
            beside(t, "turn x1", q)
            t += AFTER["keep" + last]
            beside(t, "keep x1T", q)
            t += AFTER["project"]
            beside(t, "project", q)
            t += AFTER["scale_h"]
            beside(t, "scale h", q)
            scale_h_at.append(t)
            t += AFTER["rhs1_hi"]
            beside(t, "rhs1 hi", q)
            t += AFTER["rhs1_lo"]
            beside(t, "rhs1 lo", q)
            rhs1_at.append(t)
    assert NORMS[:BLOCKS] == [(0, r) for r in range(BLOCKS)] and len(NORMS) == 2 * BLOCKS
    for v, (r, c, layers, _) in enumerate(VISITS):
        assert 1 not in layers or v * PAIRS > rhs1_at[c]

    LENT = [("rhs1", 4), ("rhs1", 8), ("rhs1", 12), ("sum1", 8)]
    until = [len(VISITS)] * SLOTS + [scale_h_at[first] // PAIRS - 2 for _, first in LENT]
    last_visit = {}
    for v, (r, c, _, loaded) in enumerate(VISITS):
        held_by = v if loaded else max(n for n in LOADS if n < v and VISITS[n][:2] == (r, c))
        last_visit[held_by] = v
    slot_of, free_after, uses = {}, {}, [-1] * U_SLOT + [U_VISIT] * 2 + [-1] * len(LENT)
    loads_into = [0] * len(until)
    for v in LOADS:
        slot = min((i for i in range(len(until)) if last_visit[v] < until[i]),
                   key=lambda i: (uses[i], -i if uses[i] >= 0 else i))
        assert uses[slot] < v
        free_after[v] = -1 if U_SLOT <= slot < SLOTS and not loads_into[slot] else uses[slot]
        uses[slot] = last_visit[v]
        loads_into[slot] += 1
        slot_of[v] = (slot, loads_into[slot])
    for v, (r, c, _, loaded) in enumerate(VISITS):
        if not loaded:
            slot_of[v] = slot_of[max(n for n in LOADS if n < v and VISITS[n][:2] == (r, c))]

    NSETS = 2

    ctx = ExitStack()
    with ctx:
        def sb(name, shape, dt=fp32):
            return ctx.enter_context(nc.sbuf_tensor(name, shape, dt))

        def ps(name, shape, dt=fp32):
            return ctx.enter_context(nc.psum_tensor(name, shape, dt))

        def sem(name):
            return ctx.enter_context(nc.semaphore(name))

        ring = sb("adj_ring", [P, SLOTS, S * ROWS])
        drop = ring[:, U_SLOT:U_SLOT + 2, :].rearrange("p s (t d) -> p (s t) d", d=D)
        rhs0 = sb("rhs_layer0", [P, KT, 2 * D], fp32r)
        with nc.sbuf_tensor("adj_in_rhs_layer1", [P, KT // 16, S * ROWS], fp32) as lent_rhs1:
            pass
        rhs1 = sb("rhs_layer1", [P, KT, 2 * D], fp32r)
        rhs1_f = rhs1[:].bitcast(fp32)
        xt = sb("x_table", [P, KT, D])
        sum1 = sb("sum_layer1", [P, KT, D])
        slots = [ring[:, i, :] for i in range(SLOTS)]
        for table, first in LENT:
            if table == "rhs1":
                slots.append(lent_rhs1[:, first // 4, :])
            else:
                slots.append(sum1[:, first * S:(first + 8) * S, :].rearrange("p t d -> p (t d)"))
        a_hi = sb("adj_hi", [P, BUFS, 2, ROWS], fp32r)
        a_hi_f = a_hi[:].bitcast(fp32)
        a_lo = sb("adj_lo", [P, BUFS, 2, ROWS], fp32r)
        acc_sb = sb("acc_sb", [P, ROWS])
        ident = sb("ident", [P, P])
        fold0 = sb("fold0", [P, D + 1])
        fold1 = sb("fold1", [P, D])
        wb = sb("w_and_b", [D + 1, D])
        sq = sb("squared", [P, S, D])
        x1T = sb("x1_turned", [D + 1, ROWS])
        d_all = sb("d_table", [P, KT])
        rsum, vsum = (sb(n, [P, NSETS, S]) for n in ("rsum", "vsum"))
        mean, var, rstd, deg, iszero, degs, dpow, nonzero = (
            sb(n, [P, S]) for n in ("mean", "var", "rstd", "deg", "iszero", "degs", "dpow", "nonzero"))
        minus_half, per_column, eps = (sb(n, [P, S]) for n in ("minus_half", "per_column", "eps"))

        acc = [ps(f"acc{i}", [P, ROWS]) for i in range(ACCS)]
        folded_ps = ps("folded_ps", [P, ROWS])
        h_ps = ps("h_ps", [P, ROWS])
        z0 = folded_ps[:, 0:S * (D + 1)].rearrange("p (s d) -> p s d", s=S)
        z1 = folded_ps[:, 0:S * D].rearrange("p (s d) -> p s d", s=S)
        h = h_ps[:, 0:S * D].rearrange("p (s d) -> p s d", s=S)

        x_in = [sem(f"x_in{i}") for i in range(PREP)]
        u_in = [sem(f"u_in{i}") for i in range(PREP)]
        w_in = sem("w_in")
        adj_in = [sem(f"adj_in{i}") for i in range(len(until))]
        out_stored = sem("out_stored")
        consts_made = sem("consts_made")
        ones_made = sem("ones_made")
        masked = sem("masked")
        shifted = sem("shifted")
        rhs0_hi = sem("rhs0_hi")
        rhs0_made = sem("rhs0_made")
        hi_made = sem("hi_made")
        lo_made = sem("lo_made")
        multiplied = sem("multiplied")
        evicted = sem("evicted")
        folded = sem("folded")
        absorbed = sem("absorbed")
        scaled = sem("scaled")
        relu_made = sem("relu_made")
        sums_made = sem("sums_made")
        cen_made = sem("cen_made")
        squared = sem("squared_made")
        vsums_made = sem("vsums_made")
        normed_made = sem("normed_made")
        d_made = sem("d_made")
        x1_turned = sem("x1_turned_made")
        x1T_made = sem("x1T_made")
        projected = sem("projected")
        hd_made = sem("hd_made")
        rhs1_hi = sem("rhs1_hi")
        rhs1_made = sem("rhs1_made")
        pool_step = sem("pool_step")

        def tiles_of(r):
            return slice(r * S, (r + 1) * S)

        def rows_of(q):
            layer, r = NORMS[q]
            return (sum1 if layer else xt)[:, tiles_of(r), :]

        block = ctx.enter_context(nc.Block())

        @block.sync
        def _(sp):
            def load_piece(i):
                piece = slice(i * PT, (i + 1) * PT)
                sp.dma_start(drop[:, piece, :], u[:, piece, :]).then_inc(u_in[i], 16)
                sp.dma_start(xt[:, piece, :], x[:, piece, :]).then_inc(x_in[i], 16)

            def store_rows(q):
                rows = tiles_of(NORMS[q][1])
                sp.wait_ge(normed_made, q + 1)
                sp.dma_start(out[:, rows, :], sum1[:, rows, :]).then_inc(out_stored, 16)

            to_store = [q for q, (layer, _) in enumerate(NORMS) if layer == 1]
            pieces = list(PIECES)
            load_piece(pieces.pop(0))
            used_slots = set()
            for n, v in enumerate(LOADS):
                slot, _ = slot_of[v]
                if U_SLOT <= slot < SLOTS and slot not in used_slots:
                    sp.wait_ge(rhs0_made, PREP)
                    used_slots.add(slot)
                while to_store and norm_at[to_store[0]] + STORE_LAG <= free_after[v] * PAIRS:
                    store_rows(to_store.pop(0))
                if free_after[v] >= 0:
                    sp.wait_ge(lo_made, (free_after[v] + 1) * PAIRS)
                sp.dma_start(slots[slot], adj[VISITS[v][0], VISITS[v][1]]).then_inc(adj_in[slot], 16)
                while pieces and PREP - len(pieces) <= (n + PIECE_LEAD) / (PIECE_PAIRS // PAIRS):
                    load_piece(pieces.pop(0))
                if n == 2:
                    sp.dma_start(wb[0:D, :], w).then_inc(w_in, 16)
                    sp.dma_start(wb[D:D + 1, :], b.rearrange("(o d) -> o d", o=1)).then_inc(w_in, 16)

            for q in to_store:
                store_rows(q)
            sp.wait_ge(out_stored, 16 * BLOCKS)

        @block.tensor
        def _(pe):
            def multiply(n, seen):
                v, half = divmod(n, PAIRS)
                r, c, layers, _ = VISITS[v]
                if half == 0:
                    piece = PIECES.index(c * S // PT) + 1
                    if 0 in layers and piece > seen["rhs0"]:
                        pe.wait_ge(rhs0_made, piece)
                        seen["rhs0"] = piece
                    if 1 in layers and c + 1 > seen["rhs1"]:
                        pe.wait_ge(rhs1_made, c + 1)
                        seen["rhs1"] = c + 1
                    for layer in layers:
                        g = product_of(v, layer)
                        before = bank_before[g]
                        if first_visit[g] == v and before:
                            pe.wait_ge(evicted, PRODUCTS.index(before) + 1)
                for part, made in ((a_hi, hi_made), (a_lo, lo_made)):
                    pe.wait_ge(made, n + 1)
                    for i in range(2):
                        k = c * S + half * 2 + i
                        for layer in layers:
                            g = product_of(v, layer)
                            rhs, to = (rhs1 if layer else rhs0), acc[bank_of[g]]
                            last = nc.tensor.matmul(
                                to[:], rhs[:, k, :], part[:, n % BUFS, i, :],
                                start=(v == first_visit[g] and half == 0 and i == 0 and part is a_hi),
                                stop=(v == final_visit[g] and half == PAIRS - 1 and i == 1 and part is a_lo))
                last.then_inc(multiplied, 1)

            def fold(j):
                f, width = (fold1, D) if PRODUCTS[j][0] else (fold0, D + 1)
                pe.wait_ge(evicted, j + 1)
                if j:
                    pe.wait_ge(absorbed, j)
                for s in range(S):
                    last = nc.tensor.matmul(folded_ps[:, s * width:(s + 1) * width], acc_sb[:, s * P:(s + 1) * P],
                                            f[:], start=True, stop=True)
                last.then_inc(folded, 1)

            def turn_x1(q):
                pe.wait_ge(normed_made, q + 1)
                if q:
                    pe.wait_ge(hd_made, q)
                for s in range(S):
                    last = nc.tensor.transpose(h_ps[0:D, s * P:(s + 1) * P], xt[:, q * S + s, :], ident[:])
                last.then_inc(x1_turned, 1)

            def project(q):
                pe.wait_ge(x1T_made, q + 1)
                for s in range(S):
                    last = nc.tensor.matmul(h_ps[:, s * D:(s + 1) * D], x1T[:, s * P:(s + 1) * P], wb[:],
                                            start=True, stop=True)
                last.then_inc(projected, 1)

            pe.wait_ge(consts_made, 4)
            pe.wait_ge(ones_made, 1)
            pe.wait_ge(w_in, 32)
            seen = {"rhs0": 0, "rhs1": 0}
            for n, beside_n in enumerate(steps):
                if n < len(VISITS) * PAIRS:
                    multiply(n, seen)
                for name, arg in beside_n:
                    if name == "fold":
                        fold(arg)
                    elif name == "turn x1":
                        turn_x1(arg)
                    elif name == "project":
                        project(arg)

        @block.scalar
        def _(act):
            def split_hi(n):
                v, half = divmod(n, PAIRS)
                slot, count = slot_of[v]
                if half == 0:
                    act.wait_ge(adj_in[slot], 16 * count)
                if n >= BUFS:
                    act.wait_ge(multiplied, n - BUFS + 1)
                nc.scalar.activation(a_hi[:, n % BUFS, :, :],
                                     slots[slot][:, half * 2 * ROWS:(half + 1) * 2 * ROWS], ACT.Copy).then_inc(hi_made, 1)

            def evict(j):
                g = PRODUCTS[j]
                act.wait_ge(multiplied, ENDS[j] + 1)
                if j:
                    act.wait_ge(folded, j)
                nc.scalar.activation(acc_sb[:], acc[bank_of[g]][:], ACT.Copy).then_inc(evicted, 1)

            def keep_x1T(q):
                act.wait_ge(x1_turned, q + 1)
                nc.scalar.activation(x1T[0:D, :], h_ps[0:D, :], ACT.Copy).then_inc(x1T_made, 1)

            def rhs1_hi_part(q):
                act.wait_ge(hd_made, q + 1)
                if ("rhs1", q) in LENT:
                    act.wait_ge(lo_made, (uses[SLOTS + LENT.index(("rhs1", q))] + 1) * PAIRS)
                nc.scalar.activation(rhs1[:, tiles_of(q), 0:D], sum1[:, tiles_of(q), :], ACT.Copy).then_inc(rhs1_hi, 1)

            def rhs0_hi_part(i):
                tiles = slice(PIECES[i] * PT, (PIECES[i] + 1) * PT)
                act.wait_ge(shifted, i + 1)
                nc.scalar.activation(rhs0[:, tiles, 0:D - 1], drop[:, tiles, 0:D - 1], ACT.Copy,
                                     scale=UNDROP).then_inc(rhs0_hi, 1)

            for n, beside_n in enumerate(steps):
                for name, arg in beside_n:
                    if name == "split rhs0":
                        rhs0_hi_part(arg)
                    elif name == "evict":
                        evict(arg)
                    elif name == "keep x1T":
                        keep_x1T(arg)
                    elif name == "rhs1 hi":
                        rhs1_hi_part(arg)
                if n < len(VISITS) * PAIRS:
                    split_hi(n)

        @block.vector
        def _(dve):
            def split_lo(n):
                v, half = divmod(n, PAIRS)
                slot, _ = slot_of[v]
                dve.wait_ge(hi_made, n + 1)
                nc.vector.tensor_tensor(a_lo[:, n % BUFS, :, :],
                                        slots[slot][:, half * 2 * ROWS:(half + 1) * 2 * ROWS].rearrange(
                                            "p (k i) -> p k i", k=2),
                                        a_hi_f[:, n % BUFS, :, :], ALU.subtract).then_inc(lo_made, 1)

            def absorb(j):
                layer, r, _ = PRODUCTS[j]
                dve.wait_ge(folded, j + 1)
                if layer == 0:
                    if r:
                        dve.wait_ge(d_made, r)
                    nc.vector.tensor_scalar(deg[:], z0[:, :, D], 1.0, None, ALU.add)
                    nc.vector.tensor_scalar(iszero[:], z0[:, :, D], 1.0, 0.0, ALU.add, ALU.is_equal)
                    nc.vector.tensor_scalar(nonzero[:], z0[:, :, D], 1.0, 0.0, ALU.add, ALU.not_equal)
                    nc.vector.tensor_tensor(xt[:, tiles_of(r), :], z0[:, :, 0:D], xt[:, tiles_of(r), :],
                                            ALU.add).then_inc(absorbed, 1)
                else:
                    nc.vector.tensor_tensor(sum1[:, tiles_of(r), :], z1[:], sum1[:, tiles_of(r), :],
                                            ALU.add).then_inc(absorbed, 1)

            def sums(q):
                layer, r = NORMS[q]
                if layer == 0:
                    dve.wait_ge(absorbed, PRODUCTS.index((0, r, 0)) + 1)
                else:
                    dve.wait_ge(scaled, q - BLOCKS + 1)
                    nc.vector.scalar_tensor_tensor(sum1[:, tiles_of(r), :], sum1[:, tiles_of(r), :], 0.0,
                                                   xt[:, tiles_of(r), :], ALU.max, ALU.add).then_inc(relu_made, 1)
                    dve.wait_ge(relu_made, q - BLOCKS + 1)
                if q >= NSETS:
                    dve.wait_ge(cen_made, q - NSETS + 1)
                nc.vector.tensor_reduce(rsum[:, q % NSETS], rows_of(q), AX.X, ALU.add).then_inc(sums_made, 1)

            def square_sums(q):
                dve.wait_ge(squared, q + 1)
                nc.vector.tensor_reduce(vsum[:, q % NSETS], sq[:], AX.X, ALU.add).then_inc(vsums_made, 1)

            def scale_h(q):
                dve.wait_ge(projected, q + 1)
                dve.wait_ge(d_made, q + 1)
                nc.vector.tensor_tensor(sum1[:, tiles_of(q), :], h[:],
                                        d_all[:, tiles_of(q)].unsqueeze(2).to_broadcast([P, S, D]),
                                        ALU.mult).then_inc(hd_made, 1)

            def rhs1_lo_part(q):
                dve.wait_ge(rhs1_hi, q + 1)
                nc.vector.tensor_tensor(rhs1[:, tiles_of(q), D:2 * D], sum1[:, tiles_of(q), :],
                                        rhs1_f[:, tiles_of(q), 0:D], ALU.subtract).then_inc(rhs1_made, 1)

            nc.vector.memset(x1T[D:D + 1, :], 1.0).then_inc(ones_made, 1)
            nc.vector.memset(rhs0[:, :, D - 1:D].bitcast(fp32), 1.0)
            nc.vector.memset(rhs0[:, :, 2 * D - 1:2 * D].bitcast(fp32), 0.0)

            def mask_x(i):
                piece = PIECES[i]
                tiles = slice(piece * PT, (piece + 1) * PT)
                dve.wait_ge(u_in[piece], 16)
                dve.wait_ge(x_in[piece], 16)
                nc.vector.scalar_tensor_tensor(drop[:, tiles, :], drop[:, tiles, :], KEEP_FROM, xt[:, tiles, :],
                                               ALU.is_ge, ALU.mult).then_inc(masked, 1)
                dve.wait_ge(masked, i + 1)
                nc.vector.tensor_tensor(drop[:, tiles, 0:D - 1], drop[:, tiles, 0:D - 1],
                                        drop[:, tiles, D - 1:D].to_broadcast([P, PT, D - 1]),
                                        ALU.subtract).then_inc(shifted, 1)

            def rhs0_lo_part(i):
                tiles = slice(PIECES[i] * PT, (PIECES[i] + 1) * PT)
                dve.wait_ge(rhs0_hi, i + 1)
                nc.vector.scalar_tensor_tensor(rhs0[:, tiles, D:2 * D - 1], drop[:, tiles, 0:D - 1], UNDROP,
                                               rhs0[:, tiles, 0:D - 1].bitcast(fp32), ALU.mult,
                                               ALU.subtract).then_inc(rhs0_made, 1)

            for n, beside_n in enumerate(steps):
                if n == 0:
                    for name, arg in beside_n:
                        if name == "mask x":
                            mask_x(arg)
                    for name, arg in beside_n:
                        if name == "split rhs0":
                            rhs0_lo_part(arg)
                if n < len(VISITS) * PAIRS:
                    split_lo(n)
                for name, arg in beside_n:
                    if n == 0:
                        break
                    if name == "mask x":
                        mask_x(arg)
                    elif name == "split rhs0":
                        rhs0_lo_part(arg)
                    elif name == "absorb":
                        absorb(arg)
                    elif name == "sums":
                        sums(arg)
                    elif name == "squares":
                        square_sums(arg)
                    elif name == "scale h":
                        scale_h(arg)
                    elif name == "rhs1 lo":
                        rhs1_lo_part(arg)

        @block.gpsimd
        def _(pool):
            def diagonal(t, cols, off):
                return nc.gpsimd.affine_select(out=t[:, 0:cols], in_=t[:, 0:cols], compare_op=ALU.not_equal,
                                               fill=1.0, base=-off, pattern=[[-1, cols]], channel_multiplier=1)

            nc.gpsimd.memset(minus_half[:], -0.5)
            nc.gpsimd.memset(per_column[:], 1.0 / D)
            nc.gpsimd.memset(eps[:], EPS)
            nc.gpsimd.memset(ident[:], 0.0)
            nc.gpsimd.memset(fold0[:], 0.0)
            nc.gpsimd.memset(fold1[:], 0.0).then_inc(consts_made, 1)
            pool.wait_ge(consts_made, 1)
            diagonal(ident, P, 0)
            diagonal(fold0, D - 1, 0)
            diagonal(fold1, D, 0).then_inc(consts_made, 1)
            pool.wait_ge(consts_made, 2)
            diagonal(fold0, D - 1, D)
            diagonal(fold1, D, D)
            ones = fold0[:, D:D + 1]
            nc.gpsimd.affine_select(out=ones, in_=ones, compare_op=ALU.not_equal, fill=1.0, base=-(D - 1),
                                    pattern=[[-1, 1]], channel_multiplier=1).then_inc(consts_made, 1)
            pool.wait_ge(consts_made, 3)
            nc.gpsimd.affine_select(out=ones, in_=ones, compare_op=ALU.not_equal, fill=1.0, base=-(2 * D - 1),
                                    pattern=[[-1, 1]], channel_multiplier=1).then_inc(consts_made, 1)

            def wide(t):
                return t.unsqueeze(2).to_broadcast([P, S, D])

            done = [0]

            def step(ins):
                ins.then_inc(pool_step, 1)
                done[0] += 1
                pool.wait_ge(pool_step, done[0])

            def scale(q):
                r = NORMS[q][1]
                pool.wait_ge(absorbed, max(j for j, g in enumerate(PRODUCTS) if g[:2] == (1, r)) + 1)
                nc.gpsimd.tensor_tensor(sum1[:, tiles_of(r), :], sum1[:, tiles_of(r), :], wide(d_all[:, tiles_of(r)]),
                                        ALU.mult).then_inc(scaled, 1)

            def centre(q):
                layer, r = NORMS[q]
                i = q % NSETS
                pool.wait_ge(sums_made, q + 1)
                step(nc.gpsimd.tensor_tensor(mean[:], rsum[:, i], per_column[:], ALU.mult))
                nc.gpsimd.tensor_tensor(rows_of(q), rows_of(q), wide(mean[:]), ALU.subtract).then_inc(cen_made, 1)
                pool.wait_ge(cen_made, q + 1)
                if q:
                    pool.wait_ge(vsums_made, q)
                nc.gpsimd.tensor_tensor(sq[:], rows_of(q), rows_of(q), ALU.mult).then_inc(squared, 1)
                if layer == 0:
                    step(nc.gpsimd.tensor_tensor(degs[:], deg[:], iszero[:], ALU.add))
                    step(nc.gpsimd.tensor_tensor(dpow[:], degs[:], minus_half[:], ALU.pow))
                    nc.gpsimd.tensor_tensor(d_all[:, tiles_of(r)], dpow[:], nonzero[:], ALU.mult).then_inc(d_made, 1)

            def normalise(q):
                layer, r = NORMS[q]
                i = q % NSETS
                pool.wait_ge(vsums_made, q + 1)
                step(nc.gpsimd.tensor_tensor(var[:], vsum[:, i], per_column[:], ALU.mult))
                step(nc.gpsimd.tensor_tensor(var[:], var[:], eps[:], ALU.add))
                step(nc.gpsimd.tensor_tensor(rstd[:], var[:], minus_half[:], ALU.pow))
                nc.gpsimd.tensor_tensor(rows_of(q), rows_of(q), wide(rstd[:]), ALU.mult).then_inc(normed_made, 1)

            for beside_n in steps:
                for name, arg in beside_n:
                    if name == "scale":
                        scale(arg)
                    elif name == "centre":
                        centre(arg)
                    elif name == "normalise":
                        normalise(arg)


_INS = ['x', 'adj', 'L0_gnn_u', 'L1_gnn_W', 'L1_gnn_b']


def kernel(**inputs):
    import numpy as _np
    import concourse.bacc as _bacc
    from concourse import mybir as _mybir
    from concourse.bass_utils import run_bass_kernel_spmd as _run

    n, d = inputs['x'].shape
    t = n // P

    def laid_out(name):
        a = _np.asarray(inputs[name])
        if name == 'adj':
            a = a.reshape(n // ROWS, ROWS, n // ROWS, ROWS // P, P).transpose(0, 2, 4, 3, 1)
            a = a.reshape(n // ROWS, n // ROWS, P, ROWS * ROWS // P)
        elif name in ('x', 'L0_gnn_u'):
            a = a.reshape(t, P, d).transpose(1, 0, 2)
        return _np.ascontiguousarray(a)

    nc = _bacc.Bacc("TRN2", target_bir_lowering=False, num_devices=1)
    arrays, args = {}, []
    for name in _INS:
        a = laid_out(name)
        arrays[f"in_{name}_dram"] = a
        args.append(nc.dram_tensor(f"in_{name}_dram", a.shape, _mybir.dt.from_np(a.dtype), kind="ExternalInput").ap())
    out = nc.dram_tensor("out_0_dram", (P, t, d), _mybir.dt.float32, kind="ExternalOutput").ap()
    two_layer_graph_resnorm(nc, *args, out)
    r = _run(nc, [arrays], core_ids=[0])
    got = _np.asarray(r.results[0]["out_0_dram"])
    return _np.ascontiguousarray(got.transpose(1, 0, 2)).reshape(n, d)
```
